# Optimizing a Trainium2 kernel written in Bass

```python
import numpy as np
import jax
import jax.numpy as jnp

def _softmax(x, axis=-1):
    return jax.nn.softmax(x, axis=axis)

def _gelu(x):
    return jax.nn.gelu(x, approximate=True)

def _silu(x):
    return jax.nn.silu(x)

def _sigmoid(x):
    return jax.nn.sigmoid(x)

def _layernorm(x, axis=-1, eps=1e-05):
    m = jnp.mean(x, axis=axis, keepdims=True)
    v = jnp.var(x, axis=axis, keepdims=True)
    return (x - m) / jnp.sqrt(v + eps)

def _scatter_add(tgt, idx, src, axis=0):
    return tgt.at[idx].add(src)

def _segment_sum(src, seg, n):
    return jax.ops.segment_sum(src, seg, n)
kernel_name = 'mk_adj_resnorm_d1_adj_r2_19b1af'

def setup_inputs(seed: int=0):
    np.random.seed(seed)
    _w = jnp.asarray

    def _rec_inputs():
        import jax
        import jax.numpy as jnp
        _gk = jax.random.key(seed)
        x = 0.0001732 + 1 * jax.random.normal(jax.random.fold_in(_gk, 1), (5120, 64), jnp.float32)
        _a = jax.random.bernoulli(jax.random.fold_in(_gk, 2), 0.00078125, (5120, 5120))
        _a = jnp.logical_or(_a, jnp.swapaxes(_a, -1, -2))
        _a = jnp.logical_or(_a, jnp.eye(5120, dtype=bool))
        _af = _a.astype(jnp.float32)
        _af = _af * jax.random.uniform(jax.random.fold_in(_gk, 3), (5120, 5120), jnp.float32, 0.05, 0.02)
        adj = _af
        return (x, adj)
    x, adj = _rec_inputs()

    def _L0_gnn_setup():
        import jax, jax.numpy as jnp
        import numpy as np
        N_USERS = 2048
        N_ITEMS = 3072
        EMB = 64
        LN_EPS = 1e-05
        key = jax.random.key(seed)
        ks = jax.random.split(key, 10)
        N = N_USERS + N_ITEMS
        ego = jax.random.normal(ks[0], (N, EMB), jnp.float32)
        adj = (jax.random.uniform(ks[1], (N, N), jnp.float32) < 0.01).astype(jnp.float32) * 0.02
        xav = float(np.sqrt(6.0 / (EMB + EMB)))
        W_u = jax.random.uniform(ks[2], (EMB, EMB), jnp.float32, -xav, xav)
        W_i = jax.random.uniform(ks[3], (EMB, EMB), jnp.float32, -xav, xav)
        diag_u = jax.random.uniform(ks[4], (N_USERS,), jnp.float32, 0.99, 1.01)
        diag_i = jax.random.uniform(ks[5], (N_ITEMS,), jnp.float32, 0.99, 1.01)
        par_u = jax.random.uniform(ks[6], (2,), jnp.float32, 0.0, 0.99)
        par_i = jax.random.uniform(ks[7], (2,), jnp.float32, 0.0, 0.99)
        ln_gamma = jnp.ones((EMB,), jnp.float32)
        ln_beta = jnp.zeros((EMB,), jnp.float32)
        return {'ego_embeddings': ego, 'adj': adj, 'W_u': W_u, 'diag_u': diag_u, 'par_u': par_u, 'W_i': W_i, 'diag_i': diag_i, 'par_i': par_i, 'ln_gamma': ln_gamma, 'ln_beta': ln_beta}
    _L0_gnn_all = _L0_gnn_setup()
    _L0_gnn_in = {k: v for k, v in _L0_gnn_all.items() if k in ('W_u', 'diag_u', 'par_u', 'W_i', 'diag_i', 'par_i', 'ln_gamma', 'ln_beta')}
    del _L0_gnn_all
    return {'x': x, 'adj': adj, 'L0_gnn_W_u': _L0_gnn_in['W_u'], 'L0_gnn_diag_u': _L0_gnn_in['diag_u'], 'L0_gnn_par_u': _L0_gnn_in['par_u'], 'L0_gnn_W_i': _L0_gnn_in['W_i'], 'L0_gnn_diag_i': _L0_gnn_in['diag_i'], 'L0_gnn_par_i': _L0_gnn_in['par_i'], 'L0_gnn_ln_gamma': _L0_gnn_in['ln_gamma'], 'L0_gnn_ln_beta': _L0_gnn_in['ln_beta']}

def reference(x, adj, L0_gnn_W_u, L0_gnn_diag_u, L0_gnn_par_u, L0_gnn_W_i, L0_gnn_diag_i, L0_gnn_par_i, L0_gnn_ln_gamma, L0_gnn_ln_beta):
    import jax
    import jax.numpy as jnp

    def _L0_gnn_ref(ego_embeddings, adj, W_u, diag_u, par_u, W_i, diag_i, par_i, ln_gamma, ln_beta):
        import jax, jax.numpy as jnp
        import numpy as np
        N_USERS = 2048
        N_ITEMS = 3072
        EMB = 64
        LN_EPS = 1e-05
        nu = diag_u.shape[0]
        res = ego_embeddings
        ego_u = ego_embeddings[:nu]
        ego_i = ego_embeddings[nu:]
        u = par_u[0] * par_u[1] * (diag_u[:, None] * ego_u @ W_u) + ego_u
        i = par_i[0] * par_i[1] * (diag_i[:, None] * ego_i @ W_i) + ego_i
        e = jnp.concatenate([u, i], axis=0)
        h = adj @ (adj.T @ e)
        mu = jnp.mean(h, axis=-1, keepdims=True)
        var = jnp.var(h, axis=-1, keepdims=True)
        out = (h - mu) * jax.lax.rsqrt(var + LN_EPS) * ln_gamma + ln_beta + res
        return out
    x = _layernorm(x + _L0_gnn_ref(x, adj, L0_gnn_W_u, L0_gnn_diag_u, L0_gnn_par_u, L0_gnn_W_i, L0_gnn_diag_i, L0_gnn_par_i, L0_gnn_ln_gamma, L0_gnn_ln_beta), axis=-1)
    return x

_drawn_inputs = setup_inputs


def setup_inputs(seed=0):
    import zlib

    import numpy as np

    out = dict(_drawn_inputs(seed))
    spreads = {'L0_gnn_ln_gamma': (1.0, 0.2), 'L0_gnn_ln_beta': (0.0, 0.1)}
    factors = {'L0_gnn_diag_u': 8.0, 'L0_gnn_W_i': 6.067, 'L0_gnn_diag_i': 8.0}
    for name, (base, spread) in spreads.items():
        noise = np.random.default_rng([zlib.crc32(name.encode()), seed]).standard_normal(out[name].shape)
        drawn = base * np.exp(spread * noise) if base else spread * noise
        out[name] = jnp.asarray(drawn.astype(out[name].dtype))
    for name, factor in factors.items():
        out[name] = (out[name] * factor).astype(out[name].dtype)
    return out
```

```python
from contextlib import ExitStack

import concourse.bass as bass
from concourse import mybir

F32 = mybir.dt.float32
ALU = mybir.AluOpType
ACT = mybir.ActivationFunctionType

P = 128
Q = 32
SLABS = 4
EPS = 1e-05



def gnn_layer(nc, x, adj, W_u, diag_u, par_u, W_i, diag_i, par_i, gamma, beta, identity, fold, out):
    N, D = x.shape
    NT = N // P
    NU = diag_u.shape[0] // P
    KEPT = 6
    RING = 3
    SLAB = N // SLABS
    BANKS = N // 2 // 512
    GROUPS = SLAB // P
    PIECES = 2
    PG = GROUPS // PIECES
    PC = SLAB // PIECES
    ROWS = 256
    R = ROWS // Q
    NB = (NT - KEPT) * P // ROWS
    TS = 4
    TW = 4 * ROWS
    TPB = ROWS // P
    assert D == 64 and NT - KEPT == 11 * RING + 1 and NB == 2 * KEPT + 5
    LOOPED = (NT - KEPT) // RING

    with ExitStack() as ctx:
        def sb(name, shape):
            return ctx.enter_context(nc.sbuf_tensor(name, shape, F32))

        def sem(name):
            return ctx.enter_context(nc.semaphore(name))

        ring = sb("ring", [P, RING * N])
        t_at = PIECES * N
        kt_at = t_at + TS * TW
        yt_sb = ring[:, t_at:t_at + BANKS * 512]
        kept = sb("kept", [P, KEPT * N])
        x_all = sb("x_all", [P, NT * D])
        y_sb = sb("y_sb", [P, 2 * BANKS * 4 * D])
        ident = sb("ident", [P, P])
        fold_sb = sb("fold_sb", [P, D])
        gamma_sb = sb("gamma_sb", [P, D])
        beta_sb = sb("beta_sb", [P, D])
        small = sb("small", [P, 2 * 512])
        xd = [small[:, s * P:(s + 1) * P] for s in range(3)]
        xt = [small[:, (3 + s) * P:(4 + s) * P] for s in range(3)]
        e_sb = [small[:, 6 * P + s * D:6 * P + (s + 1) * D] for s in range(3)]
        wz = sb("wz", [P, D + 3 * NT])
        w_sb = wz[:, 0:D]
        du = wz[:, D:D + NT]
        di = wz[:, D + NT:D + 2 * NT]
        cf = wz[:, D + 2 * NT:D + 3 * NT]
        z_sb = [wz[:, r * D:(r + 1) * D] for r in range(TPB)]
        z_k = sb("z_k", [P, D])
        z_sb = z_sb + [z_k[:, :]]
        ht_sb = sb("ht_sb", [P, (TPB + 1) * P])
        stat = sb("stat", [P, 40])
        par = stat[:, 0:4]
        eps = stat[:, 39:40]
        ss = stat[:, 0:3]
        sd = stat[:, 3:6]
        rstd = stat[:, 6:9]
        bn = [stat[:, 9 + 6 * r:15 + 6 * r] for r in range(3)]
        mv = stat[:, 27:33]
        sd2 = stat[:, 33:36]
        rstd2 = stat[:, 36:39]

        bank = [ctx.enter_context(nc.psum_tensor(f"bank{b}", [P, 512], F32)) for b in range(8)]
        xt_ps, e_ps = bank[5], bank[6]
        h_ps = [bank[0], bank[1]]
        hk_ps = bank[2]
        kt_ps = [bank[3], bank[4]]
        hp_ps = bank[5]
        junk_ps = bank[6]
        yt_back = [bank[5], bank[6], bank[7], bank[0], bank[1]]

        const_in = sem("const_in")
        diag_in = sem("diag_in")
        x_in = sem("x_in")
        panel_in = [sem(f"panel_in{s}") for s in range(RING)]
        kept_in = [sem(f"kept_in{s}") for s in range(KEPT)]
        zeroed = sem("zeroed")
        diag_t = sem("diag_t")
        factors = sem("factors")
        xd_ready = sem("xd_ready")
        xt_turned = sem("xt_turned")
        xt_ready = sem("xt_ready")
        xw_ready = sem("xw_ready")
        e_ready = sem("e_ready")
        x2_ready = sem("x2_ready")
        panel_used = sem("panel_used")
        yt_done = sem("yt_done")
        yt_out_v = sem("yt_out_v")
        yt_out_a = sem("yt_out_a")
        y_turned = sem("y_turned")
        y_out_v = sem("y_out_v")
        y_out_a = sem("y_out_a")
        raw_in = [sem(f"raw_in{q}") for q in range(PIECES)]
        t_ready = sem("t_ready")
        t_used = sem("t_used")
        ks_ready = sem("ks_ready")
        kt_turned = sem("kt_turned")
        kt_ready = sem("kt_ready")
        kt_used = sem("kt_used")
        ht_ready = sem("ht_ready")
        hp_ready = sem("hp_ready")
        ss_ready = sem("ss_ready")
        sd_ready = sem("sd_ready")
        rstd_ready = sem("rstd_ready")
        z_scaled = sem("z_scaled")
        z_ready = sem("z_ready")
        bn_ready = sem("bn_ready")
        mv_ready = sem("mv_ready")
        sd2_ready = sem("sd2_ready")
        rstd2_ready = sem("rstd2_ready")
        out_ready = sem("out_ready")
        stored = sem("stored")

        block = ctx.enter_context(nc.Block())

        adj_rows = adj.rearrange("(t p) c -> t p c", p=P)
        adj_slabs = adj.rearrange("(b r i) (g c) -> b g i r c", r=R, i=Q, g=SLABS)

        def moving(panel, k, half):
            return panel.rearrange("p (g k m h c) -> p k h g m c", g=SLABS, k=BANKS, m=2, h=2)[:, k, half]

        def of_slabs(ap):
            return ap.rearrange("p (g a j) -> p g a j", g=SLABS, j=Q)

        def by_slab(ap):
            return ap.rearrange("p (a g j) -> p g a j", g=SLABS, j=Q)

        def slot(s):
            return ring[:, s * N:(s + 1) * N]

        def kept_slot(s):
            return kept[:, s * N:(s + 1) * N]

        def y_of(group, u, half):
            at = ((2 * group + u) * 2 + half) * D
            return y_sb[:, at:at + D]

        def t_slot(n):
            return ring[:, t_at + (n % TS) * TW:t_at + (n % TS + 1) * TW]

        def kt_slot(n):
            return ring[:, kt_at + (n % 2) * 512:kt_at + (n % 2 + 1) * 512]

        def ks_slot(n):
            return small[:, (n % 2) * 512:(n % 2 + 1) * 512]

        def x_tile(t):
            return x_all[:, bass.ds(t * D, D)]

        def rounds(eng, visit):
            visit(0, 0, 0, False)
            visit(1, 1, None, True)
            with eng.Fori(1, KEPT) as i:
                visit(2 * i, 0, i, True)
                visit(2 * i + 1, 1, None, True)
            with eng.Fori(KEPT, NB // 2) as i:
                visit(2 * i, 0, None, True)
                visit(2 * i + 1, 1, None, True)
            visit(NB - 1, 0, None, True)

        @block.sync
        def _(sp):
            for s in range(RING):
                sp.dma_start(slot(s), adj_rows[s]).then_inc(panel_in[s], 16)
            with sp.Fori(1, LOOPED) as i:
                for s in range(RING):
                    sp.wait_ge(panel_used, RING * i + (s - RING + 1))
                    sp.dma_start(slot(s), adj_rows[bass.ds(RING * i + s, 1)].rearrange("a p c -> (a p) c")).then_inc(panel_in[s], 16)
            t = RING * LOOPED
            sp.wait_ge(panel_used, t - RING + 1)
            sp.dma_start(slot(0), adj_rows[t]).then_inc(panel_in[0], 16)
            for s in range(KEPT):
                sp.dma_start(kept_slot(s), adj_rows[NT - KEPT + s]).then_inc(kept_in[s], 16)

            def load(b, parity, k, after):
                for q in range(PIECES):
                    if after:
                        sp.wait_ge(t_ready, (b - 1) * GROUPS + PG * (q + 1))
                    for g in range(SLABS):
                        dst = ring[Q * g:Q * (g + 1), q * N:(q + 1) * N]
                        src = adj_slabs[bass.ds(b, 1), g, :, :, q * PC:(q + 1) * PC]
                        sp.dma_start(dst.rearrange("i (r c) -> i r c", r=R),
                                     src.rearrange("b i r c -> (b i) r c")).then_inc(raw_in[q], 16)

            sp.wait_ge(panel_used, NT - KEPT)
            rounds(sp, load)

        @block.gpsimd
        def _(pool):
            nc.gpsimd.memset(wz[:, D:D + 2 * NT], 0.0).then_inc(zeroed, 1)

            def stage(b, parity, k, after):
                if k is None:
                    return
                if not after:
                    pool.wait_ge(yt_done, BANKS)
                panel = kept[:, bass.ds(k * N, N)].rearrange("p (g n a j) -> p n g a j", g=SLABS, n=GROUPS, j=Q)
                for n in range(GROUPS):
                    if after or n >= 2:
                        pool.wait_ge(kt_turned, k * GROUPS + n - 1)
                    nc.gpsimd.tensor_copy(by_slab(ks_slot(n)), panel[:, n]).then_inc(ks_ready, 1)

            rounds(pool, stage)

        @block.scalar
        def _(act):
            act.dma_start(x_all[:, :].rearrange("p (t d) -> p t d", d=D),
                          x.rearrange("(t p) d -> p t d", p=P)).then_inc(x_in, 16)
            act.dma_start(ht_sb[0:NU, 0:P], diag_u.rearrange("(t p) -> t p", p=P)).then_inc(diag_in, 16)
            act.dma_start(ht_sb[NU:NT, 0:P], diag_i.rearrange("(t p) -> t p", p=P)).then_inc(diag_in, 16)
            act.dma_start(ident[:, :], identity).then_inc(diag_in, 16)
            act.dma_start(par[:, 0:2], par_u.rearrange("(a n) -> a n", a=1).to_broadcast([P, 2])).then_inc(const_in, 16)
            act.dma_start(par[:, 2:4], par_i.rearrange("(a n) -> a n", a=1).to_broadcast([P, 2])).then_inc(const_in, 16)
            act.dma_start(w_sb[0:D, :], W_u).then_inc(const_in, 16)
            act.dma_start(w_sb[D:2 * D, :], W_i).then_inc(const_in, 16)
            act.dma_start(gamma_sb[:, :], gamma.rearrange("(a n) -> a n", a=1).to_broadcast([P, D])).then_inc(const_in, 16)
            act.dma_start(beta_sb[:, :], beta.rearrange("(a n) -> a n", a=1).to_broadcast([P, D])).then_inc(const_in, 16)
            act.dma_start(fold_sb[:, :], fold).then_inc(const_in, 16)

            def turn_out(t, s, first=False):
                act.wait_ge(xt_turned, t + 1)
                if not first:
                    act.wait_ge(xw_ready, t - 2)
                nc.scalar.copy(xt[s], xt_ps[:, 0:P]).then_inc(xt_ready, 1)

            for s in range(3):
                turn_out(s, s, first=True)
            with act.Fori(1, NT // 3) as i:
                for s in range(3):
                    turn_out(3 * i + s, s)
            turn_out(NT - 1, (NT - 1) % 3)

            for k in range(3, BANKS):
                act.wait_ge(yt_done, k + 1)
                nc.scalar.copy(by_slab(yt_sb[:, k * 512:(k + 1) * 512]), of_slabs(bank[k][:, :])).then_inc(yt_out_a, 1)
            for k in (1, 3):
                act.wait_ge(y_turned, k + 1)
                nc.scalar.copy(y_sb[:, k * 512:(k + 1) * 512], yt_back[k][:, :]).then_inc(y_out_a, 1)

            def kept_out(k, n, early):
                act.wait_ge(kt_turned, k * GROUPS + n + 1)
                if not early:
                    act.wait_ge(kt_used, k * GROUPS + n - 1)
                nc.scalar.copy(kt_slot(n), kt_ps[n % 2][:, :]).then_inc(kt_ready, 1)

            def norm_copy(b, parity, tiles):
                act.wait_ge(t_used, (b + 1) * GROUPS)
                if tiles > TPB:
                    act.wait_ge(kt_used, (with_kept[0] + 1) * GROUPS)
                if not_first(b):
                    act.wait_ge(hp_ready, b)
                if tiles > TPB:
                    nc.scalar.copy(ht_sb[:, TPB * P:(TPB + 1) * P], hk_ps[:, 0:P])
                nc.scalar.copy(ht_sb[:, 0:ROWS], h_ps[parity][:, 0:ROWS]).then_inc(ht_ready, 1)

            def norm_first(b, tiles):
                act.wait_ge(hp_ready, b + 1)
                if not_first(b):
                    act.wait_ge(rstd_ready, b)
                for r in range(tiles):
                    last = nc.scalar.activation(junk_ps[:, r * D:(r + 1) * D], hp_ps[:, r * D:(r + 1) * D],
                                                ACT.Square, accum_out=ss[:, r:r + 1])
                last.then_inc(ss_ready, 1)
                act.wait_ge(ss_ready, b + 1)
                nc.scalar.activation(sd[:, 0:tiles], ss[:, 0:tiles], ACT.Sqrt, bias=eps,
                                     scale=1.0 / D).then_inc(sd_ready, 1)

            def norm_second(b, tiles):
                act.wait_ge(mv_ready, b + 1)
                if not_first(b):
                    act.wait_ge(rstd2_ready, b)
                nc.scalar.activation(sd2[:, 0:tiles], mv[:, 1:2 * tiles:2], ACT.Sqrt,
                                     bias=eps).then_inc(sd2_ready, 1)

            def store(b, k):
                act.wait_ge(out_ready, b + 1)
                act.dma_start(out[bass.ds(b * ROWS, ROWS), :].rearrange("(t p) d -> p t d", p=P),
                              x_all[:, bass.ds(b * TPB * D, TPB * D)].rearrange("p (t d) -> p t d", d=D)
                              ).then_inc(stored, 16)
                if k is not None:
                    act.dma_start(out[bass.ds((NT - KEPT) * P + k * P, P), :],
                                  x_tile(NT - KEPT + k)).then_inc(stored, 16)

            def evacuate(b, parity, k, after):
                prev = b - 1
                tiles = TPB + 1 if parity and with_kept[0] is not None else TPB
                if after:
                    norm_copy(prev, 1 - parity, tiles)
                for n in range(GROUPS if k is not None else 4):
                    if k is not None:
                        kept_out(k, n, early=not after and n < 2)
                    if after and n == 3:
                        norm_first(prev, tiles)
                    if after and n == (5 if k is not None else 3):
                        norm_second(prev, tiles)
                    if after and n == (8 if k is not None else 3):
                        store(prev, with_kept[0] if tiles > TPB else None)
                with_kept[0] = k

            with_kept = [None]

            def not_first(b):
                return not (isinstance(b, int) and b == 0)

            rounds(act, evacuate)
            norm_copy(NB - 1, 0, TPB)
            norm_first(NB - 1, TPB)
            norm_second(NB - 1, TPB)
            store(NB - 1, None)
            act.wait_ge(stored, 16 * (NB + KEPT))

        @block.vector
        def _(dve):
            nc.vector.memset(eps, EPS).then_inc(factors, 1)
            dve.wait_ge(const_in, 16 * 7)
            dve.wait_ge(zeroed, 1)
            nc.vector.tensor_tensor(par[:, 1:4:2], par[:, 0:4:2], par[:, 1:4:2], ALU.mult).then_inc(factors, 1)
            dve.wait_ge(factors, 2)
            nc.vector.tensor_copy(cf[:, 0:NU], par[:, 1:2].to_broadcast([P, NU]))
            nc.vector.tensor_copy(cf[:, NU:NT], par[:, 3:4].to_broadcast([P, NT - NU]))
            dve.wait_ge(diag_t, 1)
            nc.vector.tensor_copy(du[:, 0:NU], xt_ps[:, 0:NU])
            nc.vector.tensor_copy(di[:, NU:NT], xt_ps[:, NU:NT]).then_inc(factors, 1)
            dve.wait_ge(factors, 3)
            dve.wait_ge(x_in, 16)

            def embed(t, s, first=False):
                if not first:
                    dve.wait_ge(xt_turned, t - 2)
                nc.vector.tensor_scalar(xd[s][:, 0:D], x_tile(t), du[:, bass.ds(t, 1)], None, ALU.mult)
                nc.vector.tensor_scalar(xd[s][:, D:2 * D], x_tile(t), di[:, bass.ds(t, 1)], None,
                                        ALU.mult).then_inc(xd_ready, 1)
                dve.wait_ge(xw_ready, t + 1)
                if not first:
                    dve.wait_ge(panel_used, t - 2)
                nc.vector.scalar_tensor_tensor(out=e_sb[s], in0=e_ps[:, 0:D], scalar=cf[:, bass.ds(t, 1)],
                                               in1=x_tile(t), op0=ALU.mult, op1=ALU.add).then_inc(e_ready, 1)
                dve.wait_ge(e_ready, t + 1)
                nc.vector.scalar_tensor_tensor(out=x_tile(t), in0=x_tile(t), scalar=2.0, in1=beta_sb[:, :],
                                               op0=ALU.mult, op1=ALU.add).then_inc(x2_ready, 1)

            for s in range(3):
                embed(s, s, first=True)
            with dve.Fori(1, NT // 3) as i:
                for s in range(3):
                    embed(3 * i + s, s)
            embed(NT - 1, (NT - 1) % 3)

            for k in range(3):
                dve.wait_ge(yt_done, k + 1)
                nc.vector.tensor_copy(by_slab(yt_sb[:, k * 512:(k + 1) * 512]), of_slabs(bank[k][:, :])).then_inc(yt_out_v, 1)
            for k in (0, 2, 4):
                dve.wait_ge(y_turned, k + 1)
                nc.vector.tensor_copy(y_sb[:, k * 512:(k + 1) * 512], yt_back[k][:, :]).then_inc(y_out_v, 1)

            def norm_first(b, tiles):
                dve.wait_ge(sd_ready, b + 1)
                nc.vector.reciprocal(rstd[:, 0:tiles], sd[:, 0:tiles]).then_inc(rstd_ready, 1)
                dve.wait_ge(rstd_ready, b + 1)
                for r in range(tiles):
                    last = nc.vector.scalar_tensor_tensor(
                        out=z_sb[r], in0=hp_ps[:, r * D:(r + 1) * D], scalar=rstd[:, r:r + 1],
                        in1=gamma_sb[:, :], op0=ALU.mult, op1=ALU.mult)
                last.then_inc(z_scaled, 1)
                dve.wait_ge(z_scaled, b + 1)
                for r in range(tiles):
                    last = nc.vector.tensor_tensor(z_sb[r], z_sb[r], x_tile(tile_of(b, r)), ALU.add)
                last.then_inc(z_ready, 1)
                dve.wait_ge(z_ready, b + 1)
                for r in range(tiles):
                    last = nc.vector.bn_stats(bn[r], z_sb[r])
                last.then_inc(bn_ready, 1)

            def norm_mean(tiles):
                for r in range(tiles):
                    last = nc.vector.bn_aggr(mv[:, 2 * r:2 * r + 2], bn[r])
                last.then_inc(mv_ready, 1)

            def norm_second(b, tiles):
                dve.wait_ge(sd2_ready, b + 1)
                nc.vector.reciprocal(rstd2[:, 0:tiles], sd2[:, 0:tiles]).then_inc(rstd2_ready, 1)
                dve.wait_ge(rstd2_ready, b + 1)
                for r in range(tiles):
                    last = nc.vector.tensor_scalar(x_tile(tile_of(b, r)), z_sb[r], mv[:, 2 * r:2 * r + 1],
                                                   rstd2[:, r:r + 1], ALU.subtract, ALU.mult)
                last.then_inc(out_ready, 1)

            with_kept = [None]

            def tile_of(b, r):
                return TPB * b + r if r < TPB else NT - KEPT + with_kept[0]

            def turn(b, parity, k, after):
                tiles = TPB + 1 if parity and with_kept[0] is not None else TPB
                for q in range(PIECES):
                    dve.wait_ge(raw_in[q], 16 * SLABS * (b + 1))
                    raw = ring[:, q * N:(q + 1) * N].rearrange("p (r w a c) -> p w a r c", r=R, w=PG, c=Q)
                    for w in range(PG):
                        n = q * PG + w
                        if after or n >= TS:
                            dve.wait_ge(t_used, b * GROUPS + n - TS + 1)
                        if after and n == 8:
                            dve.wait_ge(bn_ready, b)
                        nc.vector.transpose(t_slot(parity * GROUPS + n).rearrange("p (a r c) -> p a r c", a=4, r=R),
                                            raw[:, w]).then_inc(t_ready, 1)
                        if after and n == 7:
                            norm_first(b - 1, tiles)
                        if after and n == 8:
                            norm_mean(tiles)
                        if after and n == 9:
                            norm_second(b - 1, tiles)
                with_kept[0] = k

            dve.wait_ge(y_turned, BANKS)
            rounds(dve, turn)
            norm_first(NB - 1, TPB)
            dve.wait_ge(bn_ready, NB)
            norm_mean(TPB)
            norm_second(NB - 1, TPB)

        @block.tensor
        def _(pe):
            pe.wait_ge(diag_in, 48)
            pe.transpose(xt_ps[:, 0:NT], ht_sb[0:NT, 0:P], ident[0:NT, 0:NT]).then_inc(diag_t, 1)

            def turn_x(t, s):
                pe.wait_ge(xd_ready, t + 1)
                if not (isinstance(t, int) and t == 0):
                    pe.wait_ge(xt_ready, t)
                pe.transpose(xt_ps[:, 0:P], xd[s], ident[:, :]).then_inc(xt_turned, 1)

            def embed(t, s):
                pe.wait_ge(xt_ready, t + 1)
                if not (isinstance(t, int) and t == 0):
                    pe.wait_ge(e_ready, t)
                pe.matmul(e_ps[:, 0:D], xt[s], w_sb, start=True, stop=True).then_inc(xw_ready, 1)

            def multiply(t, panel, s, first=False, last=False):
                pe.wait_ge(e_ready, t + 1)
                for k in range(BANKS):
                    for half in range(2):
                        mm = pe.matmul(bank[k][D * half:D * (half + 1), :], e_sb[s], moving(panel, k, half),
                                       start=first, stop=last)
                    if last:
                        mm.then_inc(yt_done, 1)
                    if k == 1 and not last:
                        turn_x(t + 1, (s + 1) % 3)
                    if k == 3 and not last:
                        embed(t + 1, (s + 1) % 3)
                if not last:
                    mm.then_inc(panel_used, 1)

            turn_x(0, 0)
            embed(0, 0)
            for s in range(RING):
                pe.wait_ge(panel_in[s], 16)
                multiply(s, slot(s), s, first=(s == 0))
            with pe.Fori(1, LOOPED) as i:
                for s in range(RING):
                    pe.wait_ge(panel_in[s], 16 * (i + 1))
                    multiply(RING * i + s, slot(s), s)
            pe.wait_ge(panel_in[0], 16 * (LOOPED + 1))
            multiply(NT - KEPT - 1, slot(0), 0)
            for s in range(KEPT):
                t = NT - KEPT + s
                pe.wait_ge(kept_in[s], 16)
                multiply(t, kept_slot(s), t % 3, last=(s == KEPT - 1))

            for k in range(BANKS):
                if k < 3:
                    pe.wait_ge(yt_out_v, k + 1)
                else:
                    pe.wait_ge(yt_out_a, k - 2)
                for a in range(4):
                    tr = pe.transpose(yt_back[k][:, a * P:(a + 1) * P], yt_sb[:, (4 * k + a) * P:(4 * k + a + 1) * P], ident[:, :])
                tr.then_inc(y_turned, 1)

            def group(b, parity, n):
                pe.wait_ge(t_ready, b * GROUPS + n + 1)
                t = t_slot(parity * GROUPS + n)
                for u in range(2):
                    for half in range(2):
                        at = (2 * half + u) * ROWS
                        mm = pe.matmul(h_ps[parity][D * half:D * (half + 1), 0:ROWS], y_of(n, u, half),
                                       t[:, at:at + ROWS], start=(n == 0 and u == 0),
                                       stop=(n == GROUPS - 1 and u == 1))
                return mm

            def kept_turn(k, n, early):
                pe.wait_ge(ks_ready, k * GROUPS + n + 1)
                if not early:
                    pe.wait_ge(kt_ready, k * GROUPS + n - 1)
                ks = ks_slot(n)
                for a in range(4):
                    tr = pe.transpose(kt_ps[n % 2][:, a * P:(a + 1) * P], ks[:, a * P:(a + 1) * P], ident[:, :])
                tr.then_inc(kt_turned, 1)

            def kept_group(k, n):
                pe.wait_ge(kt_ready, k * GROUPS + n + 1)
                for u in range(2):
                    for half in range(2):
                        at = (2 * half + u) * P
                        mm = pe.matmul(hk_ps[D * half:D * (half + 1), 0:P], y_of(n, u, half),
                                       kt_slot(n)[:, at:at + P], start=(n == 0 and u == 0),
                                       stop=(n == GROUPS - 1 and u == 1))
                mm.then_inc(kt_used, 1)

            def norm_fold(b, tiles):
                pe.wait_ge(ht_ready, b + 1)
                if not (isinstance(b, int) and b == 0):
                    pe.wait_ge(z_scaled, b)
                for r in range(tiles):
                    mm = pe.matmul(hp_ps[:, r * D:(r + 1) * D], ht_sb[:, r * P:(r + 1) * P], fold_sb[:, :],
                                   start=True, stop=True)
                mm.then_inc(hp_ready, 1)

            with_kept = [None]

            def product(b, parity, k, after):
                tiles = TPB + 1 if parity and with_kept[0] is not None else TPB
                if not (isinstance(b, int) and b < 2):
                    pe.wait_ge(ht_ready, b - 1)
                for n in range(GROUPS):
                    mm = group(b, parity, n)
                    mm.then_inc(t_used, 1)
                    if k is not None:
                        kept_turn(k, n, early=not after and n < 2)
                        if n >= 1:
                            kept_group(k, n - 1)
                    if parity and n == 0 and with_kept[0] is not None:
                        kept_group(with_kept[0], GROUPS - 1)
                    if after and n == 2:
                        norm_fold(b - 1, tiles)
                with_kept[0] = k

            pe.wait_ge(y_out_v, 3)
            pe.wait_ge(y_out_a, 2)
            rounds(pe, product)
            norm_fold(NB - 1, TPB)


_INS = ['x', 'adj', 'L0_gnn_W_u', 'L0_gnn_diag_u', 'L0_gnn_par_u', 'L0_gnn_W_i', 'L0_gnn_diag_i',
        'L0_gnn_par_i', 'L0_gnn_ln_gamma', 'L0_gnn_ln_beta']


def kernel(**inputs):
    import numpy as _np
    import concourse.bacc as _bacc
    from concourse import mybir as _mybir
    from concourse.bass_utils import run_bass_kernel_spmd as _run

    nc = _bacc.Bacc("TRN2", target_bir_lowering=False, num_devices=1, dynamic_dma_scratch_size=2048)
    given = {name: _np.ascontiguousarray(inputs[name]) for name in _INS}
    features = given['x'].shape[1]
    given['identity'] = _np.eye(128, dtype=_np.float32)
    given['fold'] = _np.tile(_np.eye(features, dtype=_np.float32) - _np.float32(1.0 / features), (2, 1))
    arrays, args = {}, []
    for name, a in given.items():
        arrays[f"in_{name}_dram"] = a
        args.append(nc.dram_tensor(f"in_{name}_dram", a.shape, _mybir.dt.from_np(a.dtype), kind="ExternalInput").ap())
    args.append(nc.dram_tensor("out_0_dram", given['x'].shape, _mybir.dt.float32, kind="ExternalOutput").ap())
    gnn_layer(nc, *args)
    r = _run(nc, [arrays], core_ids=[0])
    return r.results[0]["out_0_dram"]
```

```python
from contextlib import ExitStack

import concourse.bass as bass
from concourse import mybir

F32 = mybir.dt.float32
ALU = mybir.AluOpType
ACT = mybir.ActivationFunctionType

P = 128
Q = 32
SLABS = 4
EPS = 1e-05



def gnn_layer(nc, x, adj, weights, diags, vectors, constants, n_users, out):
    N, D = x.shape
    NT = N // P
    NU = n_users // P
    KEPT = 6
    RING = 3
    SLAB = N // SLABS
    BANKS = N // 2 // 512
    GROUPS = SLAB // P
    PIECES = 5
    PG = GROUPS // PIECES
    PC = SLAB // PIECES
    ROWS = 256
    R = ROWS // Q
    RAW = R * PC
    NBLOCKS = N // ROWS
    NB = (NT - KEPT) * P // ROWS
    TS = 4
    TW = 4 * ROWS
    TPB = ROWS // P
    assert D == 64 and NT - KEPT == 11 * RING + 1 and NB == 2 * KEPT + 5
    LOOPED = (NT - KEPT) // RING

    with ExitStack() as ctx:
        def sb(name, shape):
            return ctx.enter_context(nc.sbuf_tensor(name, shape, F32))

        def sem(name):
            return ctx.enter_context(nc.semaphore(name))

        ring = sb("ring", [P, RING * N])
        t_at = PIECES * RAW
        kt_at = t_at + TS * TW
        yt_sb = ring[:, t_at:t_at + BANKS * 512]
        kept = sb("kept", [P, KEPT * N])
        x_all = sb("x_all", [P, NT * D])
        y_sb = sb("y_sb", [P, 2 * BANKS * 4 * D])
        const_sb = sb("const_sb", [P, P + D])
        ident = const_sb[:, 0:P]
        fold_sb = const_sb[:, P:P + D]
        vec_sb = sb("vec_sb", [P, 2 * D + 4])
        gamma_sb = vec_sb[:, 0:D]
        beta_sb = vec_sb[:, D:2 * D]
        par = vec_sb[:, 2 * D:2 * D + 4]
        small = sb("small", [P, 2 * 512])
        xd = [small[:, s * P:(s + 1) * P] for s in range(3)]
        xt = [small[:, (3 + s) * P:(4 + s) * P] for s in range(3)]
        e_sb = [small[:, 6 * P + s * D:6 * P + (s + 1) * D] for s in range(3)]
        wz = sb("wz", [P, D + 3 * NT])
        w_sb = wz[:, 0:D]
        du = wz[:, D:D + NT]
        di = wz[:, D + NT:D + 2 * NT]
        cf = wz[:, D + 2 * NT:D + 3 * NT]
        z_sb = [wz[:, r * D:(r + 1) * D] for r in range(TPB)]
        z_k = sb("z_k", [P, D])
        z_sb = z_sb + [z_k[:, :]]
        ht_sb = sb("ht_sb", [P, (TPB + 1) * P])
        stat = sb("stat", [P, 40])
        par_prod = stat[:, 0:2]
        eps = stat[:, 39:40]
        ss = stat[:, 0:3]
        sd = stat[:, 3:6]
        rstd = stat[:, 6:9]
        bn = [stat[:, 9 + 6 * r:15 + 6 * r] for r in range(3)]
        mv = stat[:, 27:33]
        sd2 = stat[:, 33:36]
        rstd2 = stat[:, 36:39]

        bank = [ctx.enter_context(nc.psum_tensor(f"bank{b}", [P, 512], F32)) for b in range(8)]
        xt_ps, e_ps = bank[5], bank[6]
        h_ps = [bank[0], bank[1]]
        hk_ps = bank[2]
        kt_ps = [bank[3], bank[4]]
        hp_ps = bank[5]
        junk_ps = bank[6]
        yt_back = [bank[5], bank[6], bank[7], bank[0], bank[1]]

        const_in = sem("const_in")
        diag_in = sem("diag_in")
        x_in = sem("x_in")
        x_rest_in = sem("x_rest_in")
        panel_in = [sem(f"panel_in{s}") for s in range(RING)]
        kept_in = [sem(f"kept_in{s}") for s in range(KEPT)]
        zeroed = sem("zeroed")
        diag_t = sem("diag_t")
        factors = sem("factors")
        xd_ready = sem("xd_ready")
        xt_turned = sem("xt_turned")
        xt_ready = sem("xt_ready")
        xw_ready = sem("xw_ready")
        e_ready = sem("e_ready")
        x2_ready = sem("x2_ready")
        panel_used = sem("panel_used")
        yt_done = sem("yt_done")
        yt_out_v = sem("yt_out_v")
        yt_out_a = sem("yt_out_a")
        y_turned = sem("y_turned")
        y_out_v = sem("y_out_v")
        y_out_a = sem("y_out_a")
        raw_in = [sem(f"raw_in{q}") for q in range(PIECES)]
        t_ready = sem("t_ready")
        t_used = sem("t_used")
        ks_ready = sem("ks_ready")
        kt_turned = sem("kt_turned")
        kt_ready = sem("kt_ready")
        kt_used = sem("kt_used")
        ht_ready = sem("ht_ready")
        hp_ready = sem("hp_ready")
        ss_ready = sem("ss_ready")
        sd_ready = sem("sd_ready")
        rstd_ready = sem("rstd_ready")
        z_scaled = sem("z_scaled")
        z_ready = sem("z_ready")
        bn_ready = sem("bn_ready")
        mv_ready = sem("mv_ready")
        sd2_ready = sem("sd2_ready")
        rstd2_ready = sem("rstd2_ready")
        out_ready = sem("out_ready")
        stored = sem("stored")

        block = ctx.enter_context(nc.Block())

        adj_panels = adj.rearrange("(b p s) c -> b s p c", p=P, s=TPB)
        x_blocks = x.rearrange("(b p s) d -> p b (s d)", p=P, s=TPB)
        out_blocks = out.rearrange("(b p s) d -> p b (s d)", p=P, s=TPB)
        x_by_block = x_all[:, :].rearrange("p (b c) -> p b c", b=NBLOCKS)
        adj_slabs = adj.rearrange("(b i r) (g c) -> b g i r c", i=Q, r=R, g=SLABS)

        def moving(panel, k, half):
            return panel.rearrange("p (g k m h c) -> p k h g m c", g=SLABS, k=BANKS, m=2, h=2)[:, k, half]

        def of_slabs(ap):
            return ap.rearrange("p (g a j) -> p g a j", g=SLABS, j=Q)

        def by_slab(ap):
            return ap.rearrange("p (a g j) -> p g a j", g=SLABS, j=Q)

        def slot(s):
            return ring[:, s * N:(s + 1) * N]

        def kept_slot(s):
            return kept[:, s * N:(s + 1) * N]

        def y_of(group, u, half):
            at = ((2 * group + u) * 2 + half) * D
            return y_sb[:, at:at + D]

        def t_slot(n):
            return ring[:, t_at + (n % TS) * TW:t_at + (n % TS + 1) * TW]

        def kt_slot(n):
            return ring[:, kt_at + (n % 2) * 512:kt_at + (n % 2 + 1) * 512]

        def ks_slot(n):
            return small[:, (n % 2) * 512:(n % 2 + 1) * 512]

        def x_tile(t):
            return x_all[:, bass.ds(t * D, D)]

        def rounds(eng, visit):
            visit(0, 0, 0, False)
            visit(1, 1, None, True)
            with eng.Fori(1, KEPT) as i:
                visit(2 * i, 0, i, True)
                visit(2 * i + 1, 1, None, True)
            with eng.Fori(KEPT, NB // 2) as i:
                visit(2 * i, 0, None, True)
                visit(2 * i + 1, 1, None, True)
            visit(NB - 1, 0, None, True)

        @block.sync
        def _(sp):
            sp.dma_start(x_by_block[:, 0:2], x_blocks[:, 0:2]).then_inc(x_in, 16)
            sp.dma_start(slot(0), adj_panels[0, 0]).then_inc(panel_in[0], 16)
            sp.dma_start(slot(1), adj_panels[0, 1]).then_inc(panel_in[1], 16)
            sp.dma_start(x_by_block[:, 2:], x_blocks[:, 2:]).then_inc(x_rest_in, 16)
            sp.dma_start(slot(2), adj_panels[1, 0]).then_inc(panel_in[2], 16)
            with sp.Fori(0, (LOOPED - 1) // TPB) as i:
                for u in range(RING * TPB):
                    t = RING + u
                    sp.wait_ge(panel_used, RING * TPB * i + (t - RING + 1))
                    sp.dma_start(slot(t % RING),
                                 adj_panels[bass.ds(RING * i + t // TPB, 1), t % TPB].rearrange("b p c -> (b p) c")
                                 ).then_inc(panel_in[t % RING], 16)
            t = RING * LOOPED
            sp.wait_ge(panel_used, t - RING + 1)
            sp.dma_start(slot(0), adj_panels[t // TPB, t % TPB]).then_inc(panel_in[0], 16)
            for s in range(KEPT):
                t = NT - KEPT + s
                sp.dma_start(kept_slot(s), adj_panels[t // TPB, t % TPB]).then_inc(kept_in[s], 16)

            def load(b, parity, k, after):
                for q in range(PIECES):
                    if after:
                        sp.wait_ge(t_ready, (b - 1) * GROUPS + PG * (q + 1))
                    for g in range(SLABS):
                        dst = ring[Q * g:Q * (g + 1), q * RAW:(q + 1) * RAW]
                        src = adj_slabs[bass.ds(b, 1), g, :, :, q * PC:(q + 1) * PC]
                        sp.dma_start(dst.rearrange("i (r c) -> i r c", r=R),
                                     src.rearrange("b i r c -> (b i) r c")).then_inc(raw_in[q], 16)

            sp.wait_ge(panel_used, NT - KEPT)
            rounds(sp, load)

        @block.gpsimd
        def _(pool):
            nc.gpsimd.memset(wz[:, D:D + 2 * NT], 0.0).then_inc(zeroed, 1)

            def stage(b, parity, k, after):
                if k is None:
                    return
                if not after:
                    pool.wait_ge(yt_done, BANKS)
                panel = kept[:, bass.ds(k * N, N)].rearrange("p (g n a j) -> p n g a j", g=SLABS, n=GROUPS, j=Q)
                for n in range(GROUPS):
                    if after or n >= 2:
                        pool.wait_ge(kt_turned, k * GROUPS + n - 1)
                    nc.gpsimd.tensor_copy(by_slab(ks_slot(n)), panel[:, n]).then_inc(ks_ready, 1)

            rounds(pool, stage)

        @block.scalar
        def _(act):
            act.dma_start(ht_sb[0:NBLOCKS, 0:ROWS], diags).then_inc(diag_in, 16)
            act.dma_start(const_sb[:, :], constants).then_inc(diag_in, 16)
            act.dma_start(vec_sb[:, :], vectors.to_broadcast([P, 2 * D + 4])).then_inc(const_in, 16)
            act.dma_start(w_sb, weights).then_inc(const_in, 16)

            def turn_out(t, s, first=False):
                act.wait_ge(xt_turned, t + 1)
                if not first:
                    act.wait_ge(xw_ready, t - 2)
                nc.scalar.copy(xt[s], xt_ps[:, 0:P]).then_inc(xt_ready, 1)

            for s in range(3):
                turn_out(s, s, first=True)
            with act.Fori(1, NT // 3) as i:
                for s in range(3):
                    turn_out(3 * i + s, s)
            turn_out(NT - 1, (NT - 1) % 3)

            for k in range(3, BANKS):
                act.wait_ge(yt_done, k + 1)
                nc.scalar.copy(by_slab(yt_sb[:, k * 512:(k + 1) * 512]), of_slabs(bank[k][:, :])).then_inc(yt_out_a, 1)
            for k in (1, 3):
                act.wait_ge(y_turned, k + 1)
                nc.scalar.copy(y_sb[:, k * 512:(k + 1) * 512], yt_back[k][:, :]).then_inc(y_out_a, 1)

            def kept_out(k, n, early):
                act.wait_ge(kt_turned, k * GROUPS + n + 1)
                if not early:
                    act.wait_ge(kt_used, k * GROUPS + n - 1)
                nc.scalar.copy(kt_slot(n), kt_ps[n % 2][:, :]).then_inc(kt_ready, 1)

            def norm_copy(b, parity, tiles):
                act.wait_ge(t_used, (b + 1) * GROUPS)
                if tiles > TPB:
                    act.wait_ge(kt_used, (with_kept[0] + 1) * GROUPS)
                if not_first(b):
                    act.wait_ge(hp_ready, b)
                if tiles > TPB:
                    nc.scalar.copy(ht_sb[:, TPB * P:(TPB + 1) * P], hk_ps[:, 0:P])
                nc.scalar.copy(ht_sb[:, 0:ROWS].rearrange("p (i r) -> p r i", r=R),
                               h_ps[parity][:, 0:ROWS].rearrange("p (r i) -> p r i", r=R)).then_inc(ht_ready, 1)

            def norm_first(b, tiles):
                act.wait_ge(hp_ready, b + 1)
                if not_first(b):
                    act.wait_ge(rstd_ready, b)
                for r in range(tiles):
                    last = nc.scalar.activation(junk_ps[:, r * D:(r + 1) * D], hp_ps[:, r * D:(r + 1) * D],
                                                ACT.Square, accum_out=ss[:, r:r + 1])
                last.then_inc(ss_ready, 1)
                act.wait_ge(ss_ready, b + 1)
                nc.scalar.activation(sd[:, 0:tiles], ss[:, 0:tiles], ACT.Sqrt, bias=eps,
                                     scale=1.0 / D).then_inc(sd_ready, 1)

            def norm_second(b, tiles):
                act.wait_ge(mv_ready, b + 1)
                if not_first(b):
                    act.wait_ge(rstd2_ready, b)
                nc.scalar.activation(sd2[:, 0:tiles], mv[:, 1:2 * tiles:2], ACT.Sqrt,
                                     bias=eps).then_inc(sd2_ready, 1)

            def store(b):
                act.wait_ge(out_ready, b + 1)
                act.dma_start(out_blocks[:, bass.ds(b, 1)], x_by_block[:, bass.ds(b, 1)]).then_inc(stored, 16)
                if isinstance(b, int) and b == NB - 2:
                    act.dma_start(out_blocks[:, NB:NBLOCKS], x_by_block[:, NB:NBLOCKS]).then_inc(stored, 16)

            def evacuate(b, parity, k, after):
                prev = b - 1
                tiles = TPB + 1 if parity and with_kept[0] is not None else TPB
                if after:
                    norm_copy(prev, 1 - parity, tiles)
                for n in range(GROUPS if k is not None else 4):
                    if k is not None:
                        kept_out(k, n, early=not after and n < 2)
                    if after and n == 3:
                        norm_first(prev, tiles)
                    if after and n == (5 if k is not None else 3):
                        norm_second(prev, tiles)
                    if after and n == (8 if k is not None else 3):
                        store(prev)
                with_kept[0] = k

            with_kept = [None]

            def not_first(b):
                return not (isinstance(b, int) and b == 0)

            rounds(act, evacuate)
            norm_copy(NB - 1, 0, TPB)
            norm_first(NB - 1, TPB)
            norm_second(NB - 1, TPB)
            store(NB - 1)
            act.wait_ge(stored, 16 * (NB + 1))

        @block.vector
        def _(dve):
            nc.vector.memset(eps, EPS).then_inc(factors, 1)
            dve.wait_ge(const_in, 16 * 2)
            dve.wait_ge(zeroed, 1)
            nc.vector.tensor_tensor(par_prod, par[:, 0:4:2], par[:, 1:4:2], ALU.mult).then_inc(factors, 1)
            dve.wait_ge(factors, 2)
            nc.vector.tensor_copy(cf[:, 0:NU], par_prod[:, 0:1].to_broadcast([P, NU]))
            nc.vector.tensor_copy(cf[:, NU:NT], par_prod[:, 1:2].to_broadcast([P, NT - NU]))
            dve.wait_ge(diag_t, 1)
            diag_ps = xt_ps[:, 0:NT].rearrange("p (s b) -> p b s", s=TPB)
            nc.vector.tensor_copy(du[:, 0:NU].rearrange("p (b s) -> p b s", s=TPB), diag_ps[:, 0:NU // TPB])
            nc.vector.tensor_copy(di[:, NU:NT].rearrange("p (b s) -> p b s", s=TPB),
                                  diag_ps[:, NU // TPB:]).then_inc(factors, 1)
            dve.wait_ge(factors, 3)
            dve.wait_ge(x_in, 16)

            def embed(t, s, first=False):
                if not first:
                    dve.wait_ge(xt_turned, t - 2)
                nc.vector.tensor_scalar(xd[s][:, 0:D], x_tile(t), du[:, bass.ds(t, 1)], None, ALU.mult)
                nc.vector.tensor_scalar(xd[s][:, D:2 * D], x_tile(t), di[:, bass.ds(t, 1)], None,
                                        ALU.mult).then_inc(xd_ready, 1)
                dve.wait_ge(xw_ready, t + 1)
                if not first:
                    dve.wait_ge(panel_used, t - 2)
                nc.vector.scalar_tensor_tensor(out=e_sb[s], in0=e_ps[:, 0:D], scalar=cf[:, bass.ds(t, 1)],
                                               in1=x_tile(t), op0=ALU.mult, op1=ALU.add).then_inc(e_ready, 1)
                dve.wait_ge(e_ready, t + 1)
                nc.vector.scalar_tensor_tensor(out=x_tile(t), in0=x_tile(t), scalar=2.0, in1=beta_sb,
                                               op0=ALU.mult, op1=ALU.add).then_inc(x2_ready, 1)

            for s in range(3):
                embed(s, s, first=True)
            dve.wait_ge(x_rest_in, 16)
            with dve.Fori(1, NT // 3) as i:
                for s in range(3):
                    embed(3 * i + s, s)
            embed(NT - 1, (NT - 1) % 3)

            for k in range(3):
                dve.wait_ge(yt_done, k + 1)
                nc.vector.tensor_copy(by_slab(yt_sb[:, k * 512:(k + 1) * 512]), of_slabs(bank[k][:, :])).then_inc(yt_out_v, 1)
            for k in (0, 2, 4):
                dve.wait_ge(y_turned, k + 1)
                nc.vector.tensor_copy(y_sb[:, k * 512:(k + 1) * 512], yt_back[k][:, :]).then_inc(y_out_v, 1)

            def norm_first(b, tiles):
                dve.wait_ge(sd_ready, b + 1)
                nc.vector.reciprocal(rstd[:, 0:tiles], sd[:, 0:tiles]).then_inc(rstd_ready, 1)
                dve.wait_ge(rstd_ready, b + 1)
                for r in range(tiles):
                    last = nc.vector.scalar_tensor_tensor(
                        out=z_sb[r], in0=hp_ps[:, r * D:(r + 1) * D], scalar=rstd[:, r:r + 1],
                        in1=gamma_sb, op0=ALU.mult, op1=ALU.mult)
                last.then_inc(z_scaled, 1)
                dve.wait_ge(z_scaled, b + 1)
                for r in range(tiles):
                    last = nc.vector.tensor_tensor(z_sb[r], z_sb[r], x_tile(tile_of(b, r)), ALU.add)
                last.then_inc(z_ready, 1)
                dve.wait_ge(z_ready, b + 1)
                for r in range(tiles):
                    last = nc.vector.bn_stats(bn[r], z_sb[r])
                last.then_inc(bn_ready, 1)

            def norm_mean(tiles):
                for r in range(tiles):
                    last = nc.vector.bn_aggr(mv[:, 2 * r:2 * r + 2], bn[r])
                last.then_inc(mv_ready, 1)

            def norm_second(b, tiles):
                dve.wait_ge(sd2_ready, b + 1)
                nc.vector.reciprocal(rstd2[:, 0:tiles], sd2[:, 0:tiles]).then_inc(rstd2_ready, 1)
                dve.wait_ge(rstd2_ready, b + 1)
                for r in range(tiles):
                    last = nc.vector.tensor_scalar(x_tile(tile_of(b, r)), z_sb[r], mv[:, 2 * r:2 * r + 1],
                                                   rstd2[:, r:r + 1], ALU.subtract, ALU.mult)
                last.then_inc(out_ready, 1)

            with_kept = [None]

            def tile_of(b, r):
                return TPB * b + r if r < TPB else NT - KEPT + with_kept[0]

            def turn(b, parity, k, after):
                tiles = TPB + 1 if parity and with_kept[0] is not None else TPB
                for q in range(PIECES):
                    dve.wait_ge(raw_in[q], 16 * SLABS * (b + 1))
                    raw = ring[:, q * RAW:(q + 1) * RAW].rearrange("p (r w a c) -> p w a r c", r=R, w=PG, c=Q)
                    for w in range(PG):
                        n = q * PG + w
                        if after or n >= TS:
                            dve.wait_ge(t_used, b * GROUPS + n - TS + 1)
                        if after and n == 8:
                            dve.wait_ge(bn_ready, b)
                        nc.vector.transpose(t_slot(parity * GROUPS + n).rearrange("p (a r c) -> p a r c", a=4, r=R),
                                            raw[:, w]).then_inc(t_ready, 1)
                        if after and n == 7:
                            norm_first(b - 1, tiles)
                        if after and n == 8:
                            norm_mean(tiles)
                        if after and n == 9:
                            norm_second(b - 1, tiles)
                with_kept[0] = k

            dve.wait_ge(y_turned, BANKS)
            rounds(dve, turn)
            norm_first(NB - 1, TPB)
            dve.wait_ge(bn_ready, NB)
            norm_mean(TPB)
            norm_second(NB - 1, TPB)

        @block.tensor
        def _(pe):
            pe.wait_ge(diag_in, 32)
            for s in range(TPB):
                tr = pe.transpose(xt_ps[:, s * NBLOCKS:(s + 1) * NBLOCKS], ht_sb[0:NBLOCKS, s:ROWS:TPB],
                                  ident[0:NBLOCKS, 0:NBLOCKS])
            tr.then_inc(diag_t, 1)

            def turn_x(t, s):
                pe.wait_ge(xd_ready, t + 1)
                if not (isinstance(t, int) and t == 0):
                    pe.wait_ge(xt_ready, t)
                pe.transpose(xt_ps[:, 0:P], xd[s], ident).then_inc(xt_turned, 1)

            def embed(t, s):
                pe.wait_ge(xt_ready, t + 1)
                if not (isinstance(t, int) and t == 0):
                    pe.wait_ge(e_ready, t)
                pe.matmul(e_ps[:, 0:D], xt[s], w_sb, start=True, stop=True).then_inc(xw_ready, 1)

            def multiply(t, panel, s, first=False, last=False):
                pe.wait_ge(e_ready, t + 1)
                for k in range(BANKS):
                    for half in range(2):
                        mm = pe.matmul(bank[k][D * half:D * (half + 1), :], e_sb[s], moving(panel, k, half),
                                       start=first, stop=last)
                    if last:
                        mm.then_inc(yt_done, 1)
                    if k == 1 and not last:
                        turn_x(t + 1, (s + 1) % 3)
                    if k == 3 and not last:
                        embed(t + 1, (s + 1) % 3)
                if not last:
                    mm.then_inc(panel_used, 1)

            turn_x(0, 0)
            embed(0, 0)
            for s in range(RING):
                pe.wait_ge(panel_in[s], 16)
                multiply(s, slot(s), s, first=(s == 0))
            with pe.Fori(1, LOOPED) as i:
                for s in range(RING):
                    pe.wait_ge(panel_in[s], 16 * (i + 1))
                    multiply(RING * i + s, slot(s), s)
            pe.wait_ge(panel_in[0], 16 * (LOOPED + 1))
            multiply(NT - KEPT - 1, slot(0), 0)
            for s in range(KEPT):
                t = NT - KEPT + s
                pe.wait_ge(kept_in[s], 16)
                multiply(t, kept_slot(s), t % 3, last=(s == KEPT - 1))

            for k in range(BANKS):
                if k < 3:
                    pe.wait_ge(yt_out_v, k + 1)
                else:
                    pe.wait_ge(yt_out_a, k - 2)
                for a in range(4):
                    tr = pe.transpose(yt_back[k][:, a * P:(a + 1) * P], yt_sb[:, (4 * k + a) * P:(4 * k + a + 1) * P], ident)
                tr.then_inc(y_turned, 1)

            def group(b, parity, n):
                pe.wait_ge(t_ready, b * GROUPS + n + 1)
                t = t_slot(parity * GROUPS + n)
                for u in range(2):
                    for half in range(2):
                        at = (2 * half + u) * ROWS
                        mm = pe.matmul(h_ps[parity][D * half:D * (half + 1), 0:ROWS], y_of(n, u, half),
                                       t[:, at:at + ROWS], start=(n == 0 and u == 0),
                                       stop=(n == GROUPS - 1 and u == 1))
                return mm

            def kept_turn(k, n, early):
                pe.wait_ge(ks_ready, k * GROUPS + n + 1)
                if not early:
                    pe.wait_ge(kt_ready, k * GROUPS + n - 1)
                ks = ks_slot(n)
                for a in range(4):
                    tr = pe.transpose(kt_ps[n % 2][:, a * P:(a + 1) * P], ks[:, a * P:(a + 1) * P], ident)
                tr.then_inc(kt_turned, 1)

            def kept_group(k, n):
                pe.wait_ge(kt_ready, k * GROUPS + n + 1)
                for u in range(2):
                    for half in range(2):
                        at = (2 * half + u) * P
                        mm = pe.matmul(hk_ps[D * half:D * (half + 1), 0:P], y_of(n, u, half),
                                       kt_slot(n)[:, at:at + P], start=(n == 0 and u == 0),
                                       stop=(n == GROUPS - 1 and u == 1))
                mm.then_inc(kt_used, 1)

            def norm_fold(b, tiles):
                pe.wait_ge(ht_ready, b + 1)
                if not (isinstance(b, int) and b == 0):
                    pe.wait_ge(z_scaled, b)
                for r in range(tiles):
                    rows = slice(r, ROWS, TPB) if r < TPB else slice(ROWS, ROWS + P)
                    mm = pe.matmul(hp_ps[:, r * D:(r + 1) * D], ht_sb[:, rows], fold_sb,
                                   start=True, stop=True)
                mm.then_inc(hp_ready, 1)

            with_kept = [None]

            def product(b, parity, k, after):
                tiles = TPB + 1 if parity and with_kept[0] is not None else TPB
                if not (isinstance(b, int) and b < 2):
                    pe.wait_ge(ht_ready, b - 1)
                for n in range(GROUPS):
                    mm = group(b, parity, n)
                    mm.then_inc(t_used, 1)
                    if k is not None:
                        kept_turn(k, n, early=not after and n < 2)
                        if n >= 1:
                            kept_group(k, n - 1)
                    if parity and n == 0 and with_kept[0] is not None:
                        kept_group(with_kept[0], GROUPS - 1)
                    if after and n == 2:
                        norm_fold(b - 1, tiles)
                with_kept[0] = k

            pe.wait_ge(y_out_v, 3)
            pe.wait_ge(y_out_a, 2)
            rounds(pe, product)
            norm_fold(NB - 1, TPB)


_INS = ['x', 'adj', 'L0_gnn_W_u', 'L0_gnn_diag_u', 'L0_gnn_par_u', 'L0_gnn_W_i', 'L0_gnn_diag_i',
        'L0_gnn_par_i', 'L0_gnn_ln_gamma', 'L0_gnn_ln_beta']


def kernel(**inputs):
    import numpy as _np
    import concourse.bacc as _bacc
    from concourse import mybir as _mybir
    from concourse.bass_utils import run_bass_kernel_spmd as _run

    nc = _bacc.Bacc("TRN2", target_bir_lowering=False, num_devices=1, dynamic_dma_scratch_size=2048)
    d = {name.removeprefix('L0_gnn_'): _np.asarray(inputs[name]) for name in _INS}
    features = d['x'].shape[1]
    given = {
        'x': d['x'], 'adj': d['adj'],
        'weights': _np.concatenate([d['W_u'], d['W_i']]),
        'diags': _np.concatenate([d['diag_u'], d['diag_i']]).reshape(-1, 256),
        'vectors': _np.concatenate([d['ln_gamma'], d['ln_beta'], d['par_u'], d['par_i']])[None],
        'constants': _np.concatenate([_np.eye(128, dtype=_np.float32),
                                      _np.tile(_np.eye(features, dtype=_np.float32) - _np.float32(1.0 / features),
                                               (2, 1))], axis=1),
    }
    arrays, args = {}, []
    for name, a in given.items():
        a = _np.ascontiguousarray(a)
        arrays[f"in_{name}_dram"] = a
        args.append(nc.dram_tensor(f"in_{name}_dram", a.shape, _mybir.dt.from_np(a.dtype), kind="ExternalInput").ap())
    args.append(d['diag_u'].shape[0])
    args.append(nc.dram_tensor("out_0_dram", d['x'].shape, _mybir.dt.float32, kind="ExternalOutput").ap())
    gnn_layer(nc, *args)
    r = _run(nc, [arrays], core_ids=[0])
    return r.results[0]["out_0_dram"]
```

```python
from contextlib import ExitStack

import concourse.bass as bass
from concourse import mybir

F32 = mybir.dt.float32
ALU = mybir.AluOpType
ACT = mybir.ActivationFunctionType

P = 128
Q = 32
SLABS = 4
EPS = 1e-05



def gnn_layer(nc, x, adj, weights, diags, vectors, constants, n_users, out):
    N, D = x.shape
    NT = N // P
    NU = n_users // P
    KEPT = 8
    RINGED = NT - KEPT
    SLAB = N // SLABS
    BANKS = N // 2 // 512
    PIECE = N // BANKS
    GROUPS = SLAB // P
    PG = 2
    PIECES = GROUPS // PG
    ROWS = 256
    R = ROWS // Q
    NBLOCKS = N // ROWS
    TPB = ROWS // P
    NB = RINGED // TPB
    VISITS = NB + 1
    S = 3
    TW = 4 * ROWS
    BESIDE = ([(0, n) for n in range(7)], [(0, n) for n in range(7, 10)] + [(1, n) for n in range(4)],
              [(1, n) for n in range(4, 10)])
    ROUNDS = KEPT // 2
    TURNS = {1: range(0, 2), **{p: range(3 * p - 4, 3 * p - 1) for p in range(2, KEPT)}}
    EARLY = 2
    PP = 5
    AFTER = {0: (), 2: (0, 2), 3: (0, 2, 4)}
    assert D == 64 and NB == 3 * ROUNDS + 4 and NB % 3 == 1 and KEPT + (KEPT - EARLY) * PP == NT - 2

    with ExitStack() as ctx:
        def sb(name, shape):
            return ctx.enter_context(nc.sbuf_tensor(name, shape, F32))

        def sem(name):
            return ctx.enter_context(nc.semaphore(name))

        t_at = S * PG * P * R
        y_at = t_at + S * TW
        y_width = 2 * BANKS * 4 * D
        ring = sb("ring", [P, y_at + y_width])
        y_sb = ring[:, y_at:y_at + y_width]
        assert BANKS * PIECE <= t_at and t_at + BANKS * PIECE <= y_at + y_width
        yt_sb = [ring[:, t_at + k * 512:t_at + (k + 1) * 512] for k in range(BANKS)]
        kept = sb("kept", [P, KEPT * N])
        x_all = sb("x_all", [P, NT * D])
        const_sb = sb("const_sb", [P, P + D])
        ident = const_sb[:, 0:P]
        fold_sb = const_sb[:, P:P + D]
        vec_sb = sb("vec_sb", [P, 2 * D + 4])
        gamma_sb = vec_sb[:, 0:D]
        beta_sb = vec_sb[:, D:2 * D]
        par = vec_sb[:, 2 * D:2 * D + 4]
        small = sb("small", [P, (TPB + 1) * P + 2 * 512])
        ks_sb = small[:, 0:512]
        diag_sb = small[0:NBLOCKS, 0:ROWS]
        xd = small[:, 512:512 + P]
        xt = small[:, 512 + P:512 + 2 * P]
        e_sb = [small[:, 512 + 2 * P + s * D:512 + 2 * P + (s + 1) * D] for s in range(2)]
        ht_sb = small[:, 0:(TPB + 1) * P]
        kt_sb = [small[:, (TPB + 1) * P + s * 512:(TPB + 1) * P + (s + 1) * 512] for s in range(2)]
        wz = sb("wz", [P, 3 * D])
        w_sb = wz[:, 0:D]
        du = wz[:, D:D + NT]
        di = wz[:, D + NT:D + 2 * NT]
        cf = wz[:, D + 2 * NT:D + 3 * NT]
        assert D + 3 * NT <= 3 * D
        z_sb = [wz[:, r * D:(r + 1) * D] for r in range(3)]
        stat = sb("stat", [P, 43])
        par_prod = stat[:, 0:2]
        eps = stat[:, 39:40]
        ss = stat[:, 0:3]
        sd = stat[:, 3:6]
        rstd = stat[:, 6:9]
        bn = [stat[:, 9 + 6 * r:15 + 6 * r] for r in range(3)]
        mv = stat[:, 27:33]
        sd2 = stat[:, 33:36]
        rstd2 = stat[:, 36:39]
        shift = stat[:, 40:43]

        bank = [ctx.enter_context(nc.psum_tensor(f"bank{b}", [P, 512], F32)) for b in range(8)]
        xt_ps, e_ps = bank[5], bank[6]
        h_ps = [bank[0], bank[1], bank[2]]
        hk_ps = [bank[3], bank[4]]
        kt_ps = bank[7]
        hp_ps = bank[5]
        junk_ps = bank[6]
        yt_back = [bank[5], bank[6], bank[7], bank[0], bank[1]]

        vec_in = sem("vec_in")
        w_in = sem("w_in")
        diag_in = sem("diag_in")
        x_in = sem("x_in")
        x_rest_in = sem("x_rest_in")
        piece_in = [[sem(f"piece_in{s}_{k}") for k in range(BANKS)] for s in range(2)]
        kept_in = [sem(f"kept_in{s}") for s in range(KEPT)]
        zeroed = sem("zeroed")
        diag_t = sem("diag_t")
        factors = sem("factors")
        xd_ready = sem("xd_ready")
        xt_turned = sem("xt_turned")
        xt_ready = sem("xt_ready")
        xw_ready = sem("xw_ready")
        e_ready = sem("e_ready")
        x2_ready = sem("x2_ready")
        bank_done = sem("bank_done")
        yt_out_v = sem("yt_out_v")
        yt_out_a = sem("yt_out_a")
        y_turned = sem("y_turned")
        y_out_v = sem("y_out_v")
        y_out_a = sem("y_out_a")
        raw_in = [sem(f"raw_in{s}") for s in range(S)]
        t_ready = sem("t_ready")
        t_used = sem("t_used")
        ks_ready = sem("ks_ready")
        kt_turned = sem("kt_turned")
        kt_back = sem("kt_back")
        kt_ready = sem("kt_ready")
        kt_used = sem("kt_used")
        ht_ready = sem("ht_ready")
        hp_ready = sem("hp_ready")
        ss_ready = sem("ss_ready")
        sd_ready = sem("sd_ready")
        rstd_ready = sem("rstd_ready")
        z_scaled = sem("z_scaled")
        z_times_gamma = sem("z_times_gamma")
        z_ready = sem("z_ready")
        bn_ready = sem("bn_ready")
        mv_ready = sem("mv_ready")
        sd2_ready = sem("sd2_ready")
        rstd2_ready = sem("rstd2_ready")
        shift_ready = sem("shift_ready")
        out_ready = sem("out_ready")
        stored = sem("stored")

        block = ctx.enter_context(nc.Block())

        adj_panels = adj.rearrange("(b p s) c -> b s p c", p=P, s=TPB)
        x_blocks = x.rearrange("(b p s) d -> p b (s d)", p=P, s=TPB)
        out_blocks = out.rearrange("(b p s) d -> p b (s d)", p=P, s=TPB)
        x_by_block = x_all[:, :].rearrange("p (b c) -> p b c", b=NBLOCKS)
        adj_slabs = adj.rearrange("(b i r) (g c) -> b g i r c", i=Q, r=R, g=SLABS)

        def moving(piece, half):
            return piece.rearrange("p g (m h c) -> p h g m c", m=2, h=2)[:, half]

        def of_bank(panel, k):
            return panel.rearrange("p (g k c) -> p k g c", g=SLABS, k=BANKS)[:, k]

        def of_slabs(ap):
            return ap.rearrange("p (g a j) -> p g a j", g=SLABS, j=Q)

        def by_slab(ap):
            return ap.rearrange("p (a g j) -> p g a j", g=SLABS, j=Q)

        def slot(s, k):
            at = s * t_at + k * PIECE
            return ring[:, at:at + PIECE].rearrange("p (g c) -> p g c", g=SLABS)

        def kept_slot(s):
            return kept[:, s * N:(s + 1) * N]

        def y_of(group, u, half):
            at = ((2 * group + u) * 2 + half) * D
            return y_sb[:, at:at + D]

        def t_slot(n):
            return ring[:, t_at + (n % S) * TW:t_at + (n % S + 1) * TW]

        def x_tile(t):
            return x_all[:, bass.ds(t * D, D)]

        def raw_slot(s, size):
            return ring[:, s * PG * P * R:s * PG * P * R + size]

        def groups_beside(p):
            if isinstance(p, int) and p < KEPT:
                return list(TURNS.get(p, []))
            if isinstance(p, int) and p >= NT - 2:
                return []
            first = EARLY * GROUPS - 2 * KEPT
            return [2 * p + first, 2 * p + (first + 1)]

        def rounds(eng, visit):
            def three(i):
                for u in range(3):
                    done = None if u == 1 or (u == 0 and is_at(i, 0)) else 2 * i + (0 if u == 2 else -1)
                    visit(i, u, [(2 * i + o, o, n) for o, n in BESIDE[u]], done)

            three(0)
            with eng.Fori(1, ROUNDS) as i:
                three(i)
            for b in range(3 * ROUNDS, VISITS):
                visit(b // 3, b % 3, [], KEPT - 1 if b == 3 * ROUNDS else None)

        def halved(b):
            return isinstance(b, int) and b >= NB - 1

        def rows_of(b):
            return R // 2 if halved(b) else R

        def pieces_of(i, u):
            b = 3 * i + u
            if halved(b):
                return [(q, PIECES * (NB // 3) + 1 + u, first, groups,
                         (NB - 1) * GROUPS + (first + groups if u else PG * (q + 1 - S)))
                        for q, (first, groups) in enumerate(((0, 4), (4, 4), (8, 2)))]
            return [((PIECES * u + q) % S, PIECES * i + (PIECES * u + q) // S + 1, PG * q, PG,
                     b * GROUPS + PG * (q + 1 - S)) for q in range(PIECES)]

        def job_tiles(b, done):
            return 1 if halved(b) else TPB if done is None else TPB + 1

        def tile_of(b, r, done):
            if halved(b):
                return TPB * (NB - 1) + b - (NB - 1)
            return TPB * b + r if r < TPB else NT - KEPT + done

        def is_at(b, value):
            return isinstance(b, int) and b == value

        @block.sync
        def _(sp):
            def load_kept(s):
                t = NT - KEPT + s
                sp.dma_start(kept_slot(s), adj_panels[t // TPB, t % TPB]).then_inc(kept_in[s], 16)

            load_kept(0)
            sp.dma_start(x_by_block[:, NB:], x_blocks[:, NB:]).then_inc(x_in, 16)
            sp.dma_start(vec_sb[:, :], vectors.to_broadcast([P, 2 * D + 4])).then_inc(vec_in, 16)
            sp.dma_start(w_sb, weights).then_inc(w_in, 16)
            load_kept(1)
            load_kept(2)
            sp.dma_start(x_by_block[:, :NB], x_blocks[:, :NB]).then_inc(x_rest_in, 16)
            for s in range(3, KEPT):
                load_kept(s)
            for s in range(2):
                for k in range(BANKS):
                    sp.dma_start(slot(s, k), of_bank(adj_panels[0, s], k)).then_inc(piece_in[s][k], 16)
            with sp.Fori(1, RINGED // 2) as i:
                for s in range(2):
                    panel = adj_panels[bass.ds(i, 1), s].rearrange("b p c -> (b p) c")
                    for k in range(BANKS):
                        sp.wait_ge(bank_done, 2 * BANKS * i + (BANKS * (KEPT + s - 2) + k + 1))
                        sp.dma_start(slot(s, k), of_bank(panel, k)).then_inc(piece_in[s][k], 16)

            def load(i, u, beside, done):
                b = 3 * i + u
                for q, (s, _turns, first, groups, free) in enumerate(pieces_of(i, u)):
                    if is_at(b, 0) and q < S:
                        sp.wait_ge(bank_done, BANKS * (NT - 2) + min(PG * (q + 1), BANKS))
                    else:
                        sp.wait_ge(t_ready, free)
                    dst = raw_slot(s, groups * P * rows_of(b))
                    rows = slice(b - (NB - 1), R, TPB) if halved(b) else slice(0, R)
                    at_block = NB - 1 if halved(b) else b
                    for g in range(SLABS):
                        src = adj_slabs[bass.ds(at_block, 1), g, :, rows, P * first:P * (first + groups)]
                        sp.dma_start(dst[Q * g:Q * (g + 1)].rearrange("i (r c) -> i r c", r=rows_of(b)),
                                     src.rearrange("b i r c -> (b i) r c")).then_inc(raw_in[s], 16)

            rounds(sp, load)
            sp.wait_ge(out_ready, VISITS)
            sp.dma_start(out_blocks[:, NB - 1:NB], x_by_block[:, NB - 1:NB]).then_inc(stored, 16)
            sp.wait_ge(stored, 16 * (NB + 1))

        @block.gpsimd
        def _(pool):
            nc.gpsimd.memset(wz[:, D:D + 2 * NT], 0.0).then_inc(zeroed, 1)

            def norm_sum(b, done):
                tiles = job_tiles(b, done)
                pool.wait_ge(z_scaled, b + 1)
                z = wz[:, 0:tiles * D]
                nc.gpsimd.tensor_tensor(z.rearrange("p (t d) -> p t d", d=D), z.rearrange("p (t d) -> p t d", d=D),
                                        gamma_sb.rearrange("p (t d) -> p t d", t=1).to_broadcast([P, tiles, D]),
                                        ALU.mult).then_inc(z_times_gamma, 1)
                pool.wait_ge(z_times_gamma, b + 1)
                for r in range(tiles):
                    last = nc.gpsimd.tensor_tensor(z_sb[r], z_sb[r], x_tile(tile_of(b, r, done)), ALU.add)
                last.then_inc(z_ready, 1)

            def add(i, u, beside, done):
                b = 3 * i + u
                if not is_at(b, 0):
                    norm_sum(b - 1, done)

            rounds(pool, add)

        @block.scalar
        def _(act):
            act.dma_start(diag_sb, diags).then_inc(diag_in, 16)
            act.dma_start(const_sb[:, :], constants).then_inc(diag_in, 16)

            def turn_out(p):
                act.wait_ge(xt_turned, p + 1)
                if not is_at(p, 0):
                    act.wait_ge(xw_ready, p)
                nc.scalar.copy(xt, xt_ps[:, 0:P]).then_inc(xt_ready, 1)

            def kept_stage(k, n):
                if not (is_at(k, 0) and n == 0):
                    act.wait_ge(kt_turned, k * GROUPS + n)
                panel = kept[:, bass.ds(k * N, N)].rearrange("p (g n a j) -> p n g a j", g=SLABS, n=GROUPS, j=Q)
                nc.scalar.copy(by_slab(ks_sb), panel[:, n]).then_inc(ks_ready, 1)

            def kept_out(k, n):
                if not is_at(k, KEPT - 1):
                    kept_stage(k + (n + 1) // GROUPS, (n + 1) % GROUPS)
                elif n + 1 < GROUPS:
                    kept_stage(k, n + 1)
                else:
                    act.wait_ge(kt_turned, KEPT * GROUPS)
                panel = kept[:, bass.ds(k * N, N)].rearrange("p (a n c) -> p n a c", a=4, n=GROUPS)
                nc.scalar.copy(panel[:, n], kt_ps[:, :].rearrange("p (a c) -> p a c", a=4)).then_inc(kt_back, 1)

            for p in range(min(TURNS) + 1):
                turn_out(p)
            act.wait_ge(kept_in[0], 16)
            kept_stage(0, 0)
            for p, turns in TURNS.items():
                act.wait_ge(bank_done, BANKS * p)
                for group in turns:
                    kept_out(group // GROUPS, group % GROUPS)
                    if group == turns[0]:
                        turn_out(p + 1)

            def turn_kept(k):
                for u in range(PP):
                    kept_out(k, 2 * u)
                    turn_out(PP * k + (KEPT - PP * EARLY + u + 1))
                    kept_out(k, 2 * u + 1)

            act.wait_ge(bank_done, BANKS * KEPT)
            with act.Fori(EARLY, KEPT - 1) as k:
                turn_kept(k)
            turn_kept(KEPT - 1)
            turn_out(NT - 1)

            for k in range(3, BANKS):
                act.wait_ge(bank_done, BANKS * (NT - 1) + k + 1)
                nc.scalar.copy(by_slab(yt_sb[k]), of_slabs(bank[k][:, :])).then_inc(yt_out_a, 1)
            for k in (1, 3):
                act.wait_ge(y_turned, k + 1)
                nc.scalar.copy(y_sb[:, k * 512:(k + 1) * 512], yt_back[k][:, :]).then_inc(y_out_a, 1)

            def kept_copy(k, n):
                if not (is_at(k, 0) and n < 2):
                    act.wait_ge(kt_used, k * GROUPS + n - 1)
                panel = kept[:, bass.ds(k * N, N)].rearrange("p (a n c) -> p n a c", a=4, n=GROUPS)
                nc.scalar.copy(kt_sb[n % 2].rearrange("p (a c) -> p a c", a=4), panel[:, n]).then_inc(kt_ready, 1)

            def norm_copy(b, u, done):
                act.wait_ge(t_used, (b + 1) * GROUPS)
                if done is not None:
                    act.wait_ge(kt_used, (done + 1) * GROUPS)
                if not is_at(b, 0):
                    act.wait_ge(hp_ready, b)
                if done is not None:
                    nc.scalar.copy(ht_sb[:, ROWS:ROWS + P], hk_ps[0 if u == 1 else 1][:, 0:P])
                rows = rows_of(b) * Q
                nc.scalar.copy(ht_sb[:, 0:rows].rearrange("p (i r) -> p r i", i=Q),
                               h_ps[u][:, 0:rows].rearrange("p (r i) -> p r i", i=Q)).then_inc(ht_ready, 1)

            def norm_first(b, tiles):
                act.wait_ge(hp_ready, b + 1)
                if not is_at(b, 0):
                    act.wait_ge(rstd_ready, b)
                for r in range(tiles):
                    last = nc.scalar.activation(junk_ps[:, r * D:(r + 1) * D], hp_ps[:, r * D:(r + 1) * D],
                                                ACT.Square, accum_out=ss[:, r:r + 1])
                last.then_inc(ss_ready, 1)
                act.wait_ge(ss_ready, b + 1)
                nc.scalar.activation(sd[:, 0:tiles], ss[:, 0:tiles], ACT.Sqrt, bias=eps,
                                     scale=1.0 / D).then_inc(sd_ready, 1)

            def norm_scale(b, tiles):
                act.wait_ge(rstd_ready, b + 1)
                if not is_at(b, 0):
                    act.wait_ge(out_ready, b)
                for r in range(tiles):
                    last = nc.scalar.activation(z_sb[r], hp_ps[:, r * D:(r + 1) * D], ACT.Copy,
                                                scale=rstd[:, r:r + 1])
                last.then_inc(z_scaled, 1)

            def norm_second(b, tiles):
                act.wait_ge(mv_ready, b + 1)
                if not is_at(b, 0):
                    act.wait_ge(rstd2_ready, b)
                nc.scalar.activation(sd2[:, 0:tiles], mv[:, 1:2 * tiles:2], ACT.Sqrt,
                                     bias=eps).then_inc(sd2_ready, 1)

            def norm_last(b, done):
                act.wait_ge(shift_ready, b + 1)
                for r in range(job_tiles(b, done)):
                    last = nc.scalar.activation(x_tile(tile_of(b, r, done)), z_sb[r], ACT.Identity,
                                                bias=shift[:, r:r + 1], scale=rstd2[:, r:r + 1])
                last.then_inc(out_ready, 1)

            def store(b):
                act.wait_ge(out_ready, b + 1)
                act.dma_start(out_blocks[:, bass.ds(b, 1)], x_by_block[:, bass.ds(b, 1)]).then_inc(stored, 16)
                if is_at(b, 3 * ROUNDS - 1):
                    act.dma_start(out_blocks[:, NB:], x_by_block[:, NB:]).then_inc(stored, 16)

            def evacuate(i, u, beside, done):
                b = 3 * i + u
                before = not is_at(b, 0)
                tiles = job_tiles(b - 1, done)

                def copies(*which):
                    for k, _odd, n in beside[which[0]:which[-1] + 1]:
                        kept_copy(k, n)

                copies(0)
                if before:
                    norm_copy(b - 1, (u - 1) % 3, done)
                copies(1)
                if before:
                    norm_first(b - 1, tiles)
                copies(2, 3)
                if before:
                    norm_scale(b - 1, tiles)
                copies(4, 5)
                if before:
                    norm_second(b - 1, tiles)
                copies(6)
                if before:
                    norm_last(b - 1, done)
                if before and not is_at(b, NB):
                    store(b - 1)

            act.wait_ge(kt_back, KEPT * GROUPS)
            rounds(act, evacuate)
            norm_copy(NB, NB % 3, None)
            norm_first(NB, 1)
            norm_second(NB, 1)

        @block.vector
        def _(dve):
            nc.vector.memset(eps, EPS).then_inc(factors, 1)
            dve.wait_ge(vec_in, 16)
            dve.wait_ge(zeroed, 1)
            nc.vector.tensor_tensor(par_prod, par[:, 0:4:2], par[:, 1:4:2], ALU.mult).then_inc(factors, 1)
            dve.wait_ge(factors, 2)
            nc.vector.tensor_copy(cf[:, 0:NU], par_prod[:, 0:1].to_broadcast([P, NU]))
            nc.vector.tensor_copy(cf[:, NU:NT], par_prod[:, 1:2].to_broadcast([P, NT - NU]))
            dve.wait_ge(diag_t, 1)
            diag_ps = xt_ps[:, 0:NT].rearrange("p (s b) -> p b s", s=TPB)
            nc.vector.tensor_copy(du[:, 0:NU].rearrange("p (b s) -> p b s", s=TPB), diag_ps[:, 0:NU // TPB])
            nc.vector.tensor_copy(di[:, NU:NT].rearrange("p (b s) -> p b s", s=TPB),
                                  diag_ps[:, NU // TPB:]).then_inc(factors, 1)
            dve.wait_ge(factors, 3)
            dve.wait_ge(x_in, 16)

            def embed(p, t, s):
                if not is_at(p, 0):
                    dve.wait_ge(xt_turned, p)
                nc.vector.tensor_scalar(xd[:, 0:D], x_tile(t), du[:, bass.ds(t, 1)], None, ALU.mult)
                nc.vector.tensor_scalar(xd[:, D:2 * D], x_tile(t), di[:, bass.ds(t, 1)], None,
                                        ALU.mult).then_inc(xd_ready, 1)
                dve.wait_ge(xw_ready, p + 1)
                if not (isinstance(p, int) and p < 2):
                    dve.wait_ge(bank_done, BANKS * p - BANKS)
                nc.vector.scalar_tensor_tensor(out=e_sb[s], in0=e_ps[:, 0:D], scalar=cf[:, bass.ds(t, 1)],
                                               in1=x_tile(t), op0=ALU.mult, op1=ALU.add).then_inc(e_ready, 1)
                dve.wait_ge(e_ready, p + 1)
                nc.vector.scalar_tensor_tensor(out=x_tile(t), in0=x_tile(t), scalar=2.0, in1=beta_sb,
                                               op0=ALU.mult, op1=ALU.add).then_inc(x2_ready, 1)

            for p in range(KEPT):
                embed(p, NT - KEPT + p, p % 2)
            dve.wait_ge(x_rest_in, 16)
            with dve.Fori(0, RINGED // 2) as i:
                for s in range(2):
                    embed(2 * i + (KEPT + s), 2 * i + s, s)

            for k in range(3):
                dve.wait_ge(bank_done, BANKS * (NT - 1) + k + 1)
                nc.vector.tensor_copy(by_slab(yt_sb[k]), of_slabs(bank[k][:, :])).then_inc(yt_out_v, 1)
            dve.wait_ge(bank_done, BANKS * NT)
            for k in (0, 2, 4):
                dve.wait_ge(y_turned, k + 1)
                nc.vector.tensor_copy(y_sb[:, k * 512:(k + 1) * 512], yt_back[k][:, :]).then_inc(y_out_v, 1)

            def norm_first(b, tiles):
                dve.wait_ge(sd_ready, b + 1)
                nc.vector.reciprocal(rstd[:, 0:tiles], sd[:, 0:tiles]).then_inc(rstd_ready, 1)

            def norm_stats(b, tiles):
                dve.wait_ge(z_ready, b + 1)
                for r in range(tiles):
                    last = nc.vector.bn_stats(bn[r], z_sb[r])
                last.then_inc(bn_ready, 1)

            def norm_mean(tiles):
                for r in range(tiles):
                    last = nc.vector.bn_aggr(mv[:, 2 * r:2 * r + 2], bn[r])
                last.then_inc(mv_ready, 1)

            def norm_second(b, tiles):
                dve.wait_ge(sd2_ready, b + 1)
                nc.vector.reciprocal(rstd2[:, 0:tiles], sd2[:, 0:tiles]).then_inc(rstd2_ready, 1)
                dve.wait_ge(rstd2_ready, b + 1)
                nc.vector.scalar_tensor_tensor(out=shift[:, 0:tiles], in0=mv[:, 0:2 * tiles:2], scalar=-1.0,
                                               in1=rstd2[:, 0:tiles], op0=ALU.mult, op1=ALU.mult
                                               ).then_inc(shift_ready, 1)

            def turn(i, u, beside, done):
                b = 3 * i + u
                first, stats, mean, second = (5, 7, 8, 9) if beside else (4, 6, 7, 8)
                if is_at(b, NB - 1):
                    first, stats, mean, second = 5, 8, 9, 9
                if is_at(b, NB):
                    first, stats, mean, second = 5, 7, None, 9
                tiles = job_tiles(b - 1, done)
                rows = rows_of(b)

                def norm_behind(n):
                    if is_at(b, 0):
                        return
                    if n == first:
                        norm_first(b - 1, tiles)
                    if n == stats:
                        norm_stats(b - 1, tiles)
                    if n == stats and mean is None:
                        dve.wait_ge(bn_ready, b)
                        norm_mean(tiles)
                    if n == mean:
                        norm_mean(tiles)
                    if n == second:
                        norm_second(b - 1, tiles)

                for s, turns, start, groups, _free in pieces_of(i, u):
                    dve.wait_ge(raw_in[s], 16 * SLABS * turns)
                    raw = raw_slot(s, groups * P * rows).rearrange("p (r w a c) -> p w a r c", r=rows, w=groups, c=Q)
                    for n in range(start, start + groups):
                        if not (is_at(b, 0) and n < S):
                            dve.wait_ge(t_used, b * GROUPS + n - S + 1)
                        if not is_at(b, 0) and n == mean:
                            dve.wait_ge(bn_ready, b)
                        turned = t_slot(GROUPS * u + n)[:, 0:rows * P].rearrange("p (a r c) -> p a r c", a=4, r=rows)
                        nc.vector.transpose(turned, raw[:, n - start]).then_inc(t_ready, 1)
                        norm_behind(n)

            dve.wait_ge(y_turned, BANKS)
            rounds(dve, turn)

            norm_first(NB, 1)
            dve.wait_ge(out_ready, NB)
            dve.wait_ge(rstd_ready, VISITS)
            nc.vector.scalar_tensor_tensor(out=z_sb[0], in0=hp_ps[:, 0:D], scalar=rstd[:, 0:1], in1=gamma_sb,
                                           op0=ALU.mult, op1=ALU.mult).then_inc(z_scaled, 1)
            dve.wait_ge(z_scaled, VISITS)
            last_tile = x_tile(tile_of(NB, 0, None))
            nc.vector.tensor_tensor(z_sb[0], z_sb[0], last_tile, ALU.add).then_inc(z_ready, 1)
            norm_stats(NB, 1)
            dve.wait_ge(bn_ready, VISITS)
            norm_mean(1)
            dve.wait_ge(sd2_ready, VISITS)
            nc.vector.reciprocal(rstd2[:, 0:1], sd2[:, 0:1]).then_inc(rstd2_ready, 1)
            dve.wait_ge(rstd2_ready, VISITS)
            nc.vector.tensor_scalar(last_tile, z_sb[0], mv[:, 0:1], rstd2[:, 0:1], ALU.subtract,
                                    ALU.mult).then_inc(out_ready, 1)

        @block.tensor
        def _(pe):
            pe.wait_ge(diag_in, 32)
            for s in range(TPB):
                tr = pe.transpose(xt_ps[:, s * NBLOCKS:(s + 1) * NBLOCKS], diag_sb[:, s:ROWS:TPB],
                                  ident[0:NBLOCKS, 0:NBLOCKS])
            tr.then_inc(diag_t, 1)

            def turn_x(p):
                pe.wait_ge(xd_ready, p + 1)
                if not is_at(p, 0):
                    pe.wait_ge(xt_ready, p)
                pe.transpose(xt_ps[:, 0:P], xd, ident).then_inc(xt_turned, 1)

            def embed(p):
                pe.wait_ge(xt_ready, p + 1)
                if not is_at(p, 0):
                    pe.wait_ge(e_ready, p)
                pe.matmul(e_ps[:, 0:D], xt, w_sb, start=True, stop=True).then_inc(xw_ready, 1)

            def kept_turn(group):
                pe.wait_ge(ks_ready, group + 1)
                if not is_at(group, 0):
                    pe.wait_ge(kt_back, group)
                for a in range(4):
                    tr = pe.transpose(kt_ps[:, a * P:(a + 1) * P], ks_sb[:, a * P:(a + 1) * P], ident)
                tr.then_inc(kt_turned, 1)

            def multiply(p, pieces, s, landed=None, last=False):
                pe.wait_ge(e_ready, p + 1)
                turns = groups_beside(p)
                for k in range(BANKS):
                    if landed is not None:
                        pe.wait_ge(piece_in[s][k], landed)
                    for half in range(2):
                        mm = pe.matmul(bank[k][D * half:D * (half + 1), :], e_sb[s], moving(pieces[k], half),
                                       start=is_at(p, 0), stop=last)
                    mm.then_inc(bank_done, 1)
                    if k == 1 and not last:
                        turn_x(p + 1)
                    if k == 3 and not last:
                        embed(p + 1)
                    if k in AFTER[len(turns)]:
                        kept_turn(turns[AFTER[len(turns)].index(k)])

            turn_x(0)
            pe.wait_ge(w_in, 16)
            embed(0)
            for p in range(KEPT):
                pe.wait_ge(kept_in[p], 16)
                multiply(p, [of_bank(kept_slot(p), k) for k in range(BANKS)], p % 2)

            def two_panels(i):
                for s in range(2):
                    multiply(2 * i + (KEPT + s), [slot(s, k) for k in range(BANKS)], s, 16 * (i + 1),
                             last=is_at(i, RINGED // 2 - 1) and s == 1)

            with pe.Fori(0, RINGED // 2 - 1) as i:
                two_panels(i)
            two_panels(RINGED // 2 - 1)

            for k in range(BANKS):
                if k < 3:
                    pe.wait_ge(yt_out_v, k + 1)
                else:
                    pe.wait_ge(yt_out_a, k - 2)
                if k == 2:
                    pe.wait_ge(kt_back, KEPT * GROUPS)
                for a in range(4):
                    tr = pe.transpose(yt_back[k][:, a * P:(a + 1) * P], yt_sb[k][:, a * P:(a + 1) * P], ident)
                tr.then_inc(y_turned, 1)

            def group(b, u, n):
                pe.wait_ge(t_ready, b * GROUPS + n + 1)
                rows = rows_of(b) * Q
                for v in range(2):
                    for half in range(2):
                        at = (2 * half + v) * rows
                        mm = pe.matmul(h_ps[u][D * half:D * (half + 1), 0:rows], y_of(n, v, half),
                                       t_slot(GROUPS * u + n)[:, at:at + rows], start=(n == 0 and v == 0),
                                       stop=(n == GROUPS - 1 and v == 1))
                mm.then_inc(t_used, 1)

            def kept_group(b, k, odd, n):
                pe.wait_ge(kt_ready, k * GROUPS + n + 1)
                if n == 0 and not (isinstance(b, int) and b < 3):
                    pe.wait_ge(ht_ready, b - 1)
                for v in range(2):
                    for half in range(2):
                        at = (2 * half + v) * P
                        mm = pe.matmul(hk_ps[odd][D * half:D * (half + 1), 0:P], y_of(n, v, half),
                                       kt_sb[n % 2][:, at:at + P], start=(n == 0 and v == 0),
                                       stop=(n == GROUPS - 1 and v == 1))
                mm.then_inc(kt_used, 1)

            def norm_fold(b, done):
                pe.wait_ge(ht_ready, b + 1)
                if not is_at(b, 0):
                    pe.wait_ge(z_scaled, b)
                tiles = [slice(0, P)] if halved(b) else [slice(r, ROWS, TPB) for r in range(TPB)]
                if done is not None:
                    tiles.append(slice(ROWS, ROWS + P))
                for r, rows in enumerate(tiles):
                    mm = pe.matmul(hp_ps[:, r * D:(r + 1) * D], ht_sb[:, rows], fold_sb, start=True, stop=True)
                mm.then_inc(hp_ready, 1)

            def product(i, u, beside, done):
                b = 3 * i + u
                if not (isinstance(b, int) and b < 3):
                    pe.wait_ge(ht_ready, b - 2)
                behind = {0: (), 6: (1, 3, 4, 6, 7, 9), 7: (1, 2, 4, 5, 7, 8, 9)}[len(beside)]
                for n in range(GROUPS):
                    group(b, u, n)
                    if n == 1 and not is_at(b, 0):
                        norm_fold(b - 1, done)
                    if n in behind:
                        kept_group(b, *beside[behind.index(n)])

            pe.wait_ge(y_out_v, 3)
            pe.wait_ge(y_out_a, 2)
            rounds(pe, product)
            norm_fold(NB, None)


_INS = ['x', 'adj', 'L0_gnn_W_u', 'L0_gnn_diag_u', 'L0_gnn_par_u', 'L0_gnn_W_i', 'L0_gnn_diag_i',
        'L0_gnn_par_i', 'L0_gnn_ln_gamma', 'L0_gnn_ln_beta']


def kernel(**inputs):
    import numpy as _np
    import concourse.bacc as _bacc
    from concourse import mybir as _mybir
    from concourse.bass_utils import run_bass_kernel_spmd as _run

    nc = _bacc.Bacc("TRN2", target_bir_lowering=False, num_devices=1, dynamic_dma_scratch_size=64)
    d = {name.removeprefix('L0_gnn_'): _np.asarray(inputs[name]) for name in _INS}
    features = d['x'].shape[1]
    given = {
        'x': d['x'], 'adj': d['adj'],
        'weights': _np.concatenate([d['W_u'], d['W_i']]),
        'diags': _np.concatenate([d['diag_u'], d['diag_i']]).reshape(-1, 256),
        'vectors': _np.concatenate([d['ln_gamma'], d['ln_beta'], d['par_u'], d['par_i']])[None],
        'constants': _np.concatenate([_np.eye(128, dtype=_np.float32),
                                      _np.tile(_np.eye(features, dtype=_np.float32) - _np.float32(1.0 / features),
                                               (2, 1))], axis=1),
    }
    arrays, args = {}, []
    for name, a in given.items():
        a = _np.ascontiguousarray(a)
        arrays[f"in_{name}_dram"] = a
        args.append(nc.dram_tensor(f"in_{name}_dram", a.shape, _mybir.dt.from_np(a.dtype), kind="ExternalInput").ap())
    args.append(d['diag_u'].shape[0])
    args.append(nc.dram_tensor("out_0_dram", d['x'].shape, _mybir.dt.float32, kind="ExternalOutput").ap())
    gnn_layer(nc, *args)
    r = _run(nc, [arrays], core_ids=[0])
    return r.results[0]["out_0_dram"]
```
